# Optimizing a Trainium2 kernel written in Bass

```python
import numpy as np
import jax
import jax.numpy as jnp

def _softmax(x, axis=-1):
    return jax.nn.softmax(x, axis=axis)

def _gelu(x):
    return jax.nn.gelu(x, approximate=True)

def _silu(x):
    return jax.nn.silu(x)

def _sigmoid(x):
    return jax.nn.sigmoid(x)

def _layernorm(x, axis=-1, eps=1e-05):
    m = jnp.mean(x, axis=axis, keepdims=True)
    v = jnp.var(x, axis=axis, keepdims=True)
    return (x - m) / jnp.sqrt(v + eps)

def _scatter_add(tgt, idx, src, axis=0):
    return tgt.at[idx].add(src)

def _segment_sum(src, seg, n):
    return jax.ops.segment_sum(src, seg, n)
kernel_name = 'mk_adaln_ffn_d1_seqx_r8_30df48'

def setup_inputs(seed: int=0):
    np.random.seed(seed)
    _w = jnp.asarray

    def _rec_inputs():
        import jax
        import jax.numpy as jnp
        _rk = jax.random.key(seed)
        x = -7.109e-05 + 0.9999 * jax.random.normal(jax.random.fold_in(_rk, 1), (8, 128, 512), jnp.float32)
        _lenS = 128 - jax.random.randint(jax.random.fold_in(_rk, 7), (8,), 0, max(1, 128 // 4) + 1, jnp.int32)
        _lenS2 = 128 - jax.random.randint(jax.random.fold_in(_rk, 8), (8,), 0, max(1, 128 // 4) + 1, jnp.int32)
        itok_B_0_15 = jax.random.randint(jax.random.fold_in(_rk, 11), (8,), 0, 16, jnp.int32)
        return (x, itok_B_0_15)
    x, itok_B_0_15 = _rec_inputs()

    def _L0_cond_setup():
        import jax, jax.numpy as jnp
        import numpy as np
        SCALING = 16.0 / 16
        key = jax.random.key(seed)
        k1, k2, k3, k4, k5 = jax.random.split(key, 5)
        B, S, D_IN, D_OUT, R, N_ADPT = (8, 256, 512, 512, 16, 16)
        x = jax.random.normal(k1, (B, S, D_IN), dtype=jnp.float32)
        adapter_indices = jax.random.randint(k2, (B,), 0, N_ADPT, dtype=jnp.int32)
        W = jax.random.normal(k3, (D_IN, D_OUT), dtype=jnp.float32) * 0.02
        lora_A = jax.random.normal(k4, (N_ADPT, D_IN, R), dtype=jnp.float32) * 0.02
        lora_B = jax.random.normal(k5, (N_ADPT, R, D_OUT), dtype=jnp.float32) * 0.02
        return {'x': x, 'adapter_indices': adapter_indices, 'W': W, 'lora_A': lora_A, 'lora_B': lora_B}
    _L0_cond_all = _L0_cond_setup()
    _L0_cond_in = {k: v for k, v in _L0_cond_all.items() if k in ('W', 'lora_A', 'lora_B')}
    del _L0_cond_all

    def _L0_ffn_setup():
        import jax, jax.numpy as jnp
        import numpy as np
        BATCH, TOK, DIM, OUT = (4, 256, 512, 512)
        E, R, TOP_K = (8, 16, 2)
        SCALING = 16.0 / R
        key = jax.random.key(seed)
        ks = jax.random.split(key, 6)
        return {'x': jax.random.normal(ks[0], (BATCH, TOK, DIM), dtype=jnp.float32), 'W_base': jax.random.normal(ks[1], (OUT, DIM), dtype=jnp.float32) / np.sqrt(DIM), 'b_base': jax.random.normal(ks[2], (OUT,), dtype=jnp.float32) * 0.01, 'W_gate': jax.random.normal(ks[3], (E, DIM), dtype=jnp.float32) * 0.01, 'A': jax.random.normal(ks[4], (E, R, DIM), dtype=jnp.float32) / np.sqrt(DIM), 'B': jax.random.normal(ks[5], (OUT, OUT // OUT * R * 0 + R), dtype=jnp.float32)[None].repeat(E, 0) * 0.0 + jax.random.normal(ks[5], (E, OUT, R), dtype=jnp.float32) * 0.02}
    _L0_ffn_all = _L0_ffn_setup()
    _L0_ffn_in = {k: v for k, v in _L0_ffn_all.items() if k in ('W_base', 'b_base', 'W_gate', 'A', 'B')}
    del _L0_ffn_all
    return {'x': x, 'itok_B_0_15': itok_B_0_15, 'L0_cond_W': _L0_cond_in['W'], 'L0_cond_lora_A': _L0_cond_in['lora_A'], 'L0_cond_lora_B': _L0_cond_in['lora_B'], 'L0_ffn_W_base': _L0_ffn_in['W_base'], 'L0_ffn_b_base': _L0_ffn_in['b_base'], 'L0_ffn_W_gate': _L0_ffn_in['W_gate'], 'L0_ffn_A': _L0_ffn_in['A'], 'L0_ffn_B': _L0_ffn_in['B']}

def reference(x, itok_B_0_15, L0_cond_W, L0_cond_lora_A, L0_cond_lora_B, L0_ffn_W_base, L0_ffn_b_base, L0_ffn_W_gate, L0_ffn_A, L0_ffn_B):
    import jax
    import jax.numpy as jnp

    def _L0_cond_ref(x, adapter_indices, W, lora_A, lora_B):
        import jax, jax.numpy as jnp
        import numpy as np
        SCALING = 16.0 / 16
        base_out = jnp.einsum('bsi,io->bso', x, W)
        A = lora_A[adapter_indices]
        Bm = lora_B[adapter_indices]
        xr = jnp.einsum('bsi,bir->bsr', x, A)
        lora_out = jnp.einsum('bsr,bro->bso', xr, Bm)
        return base_out + lora_out * SCALING

    def _L0_ffn_ref(x, W_base, b_base, W_gate, A, B):
        import jax, jax.numpy as jnp
        import numpy as np
        BATCH, TOK, DIM, OUT = (4, 256, 512, 512)
        E, R, TOP_K = (8, 16, 2)
        SCALING = 16.0 / R
        result = jnp.einsum('bnd,od->bno', x, W_base) + b_base
        logits = jnp.einsum('bnd,ed->bne', x, W_gate)
        probs = jax.nn.softmax(logits.astype(jnp.float32), axis=-1)
        top_p, top_i = jax.lax.top_k(probs, TOP_K)
        top_p = top_p / jnp.sum(top_p, axis=-1, keepdims=True)
        top_p = top_p.astype(x.dtype)
        route_w = jnp.sum(jax.nn.one_hot(top_i, E, dtype=x.dtype) * top_p[..., None], axis=-2)
        h = jnp.einsum('bnd,erd->bner', x, A)
        hw = h * route_w[..., None]
        delta = jnp.einsum('bner,eor->bno', hw, B)
        return result + delta * SCALING
    x = x + _L0_ffn_ref(_L0_cond_ref(x, itok_B_0_15, L0_cond_W, L0_cond_lora_A, L0_cond_lora_B), L0_ffn_W_base, L0_ffn_b_base, L0_ffn_W_gate, L0_ffn_A, L0_ffn_B)
    return x

_drawn_inputs = setup_inputs


def setup_inputs(seed=0):
    import zlib

    import numpy as np

    out = dict(_drawn_inputs(seed))
    spreads = {}
    factors = {'L0_ffn_b_base': 6.242, 'L0_ffn_W_gate': 7.537}
    for name, (base, spread) in spreads.items():
        noise = np.random.default_rng([zlib.crc32(name.encode()), seed]).standard_normal(out[name].shape)
        drawn = base * np.exp(spread * noise) if base else spread * noise
        out[name] = jnp.asarray(drawn.astype(out[name].dtype))
    for name, factor in factors.items():
        out[name] = (out[name] * factor).astype(out[name].dtype)
    return out
```

```python
from contextlib import ExitStack

import concourse.bass as bass
from concourse import mybir

F32 = mybir.dt.float32
F32R = mybir.dt.float32r
U32 = mybir.dt.uint32
ALU = mybir.AluOpType
ACT = mybir.ActivationFunctionType

P = 128
NT = 8
D = 512
KC = D // P
R = 16
NA = 16
E = 8
ER = E * R
GH = E + ER
WIDE = D + GH
TOP = 2
ROWS = 4 * R + 2
DMA = 16


def adaln_ffn_kernel(nc, x_t, itok, fold_in, lora, ffn_b, bias, out):
    ctx = ExitStack()
    with ctx:
        def sb(name, shape, dt=F32):
            return ctx.enter_context(nc.sbuf_tensor(name, shape, dt))

        def sem(name):
            return ctx.enter_context(nc.semaphore(name))

        w_raw = sb("w_raw", [P, KC, D + GH + D])
        lora_raw = sb("lora_raw", [P, NT, 2 * KC * R])
        x_raw = sb("x_raw", [P, NT, KC, P])
        ffn_b_raw = sb("ffn_b_raw", [P, D])
        bias_raw = sb("bias_raw", [1, D])
        wt_hi = sb("wt_hi", [P, KC, D], F32R)
        wt_lo = sb("wt_lo", [P, KC, D], F32R)
        wb_hi = sb("wb_hi", [P, KC, D], F32R)
        wb_lo = sb("wb_lo", [P, KC, D], F32R)
        lb_raw = sb("lb_raw", [P, KC, R, NT])
        lb_hi = sb("lb_hi", [P, KC, R, NT], F32R)
        lb_lo = sb("lb_lo", [P, KC, R, NT], F32R)
        x_hi = sb("x_hi", [P, NT, KC, P], F32R)
        x_lo = sb("x_lo", [P, NT, KC, P], F32R)
        ffn_b_hi = sb("ffn_b_hi", [P, D], F32R)
        ffn_b_lo = sb("ffn_b_lo", [P, D], F32R)
        bias_hi = sb("bias_hi", [1, D], F32R)
        bias_lo = sb("bias_lo", [1, D], F32R)
        c_hi = sb("c_hi", [P, KC, D], F32R)
        c_lo = sb("c_lo", [P, KC, D], F32R)
        c_gh = sb("c_gh", [P, KC, R + GH + R])
        bw_hi = sb("bw_hi", [P, WIDE], F32R)
        bw_lo = sb("bw_lo", [P, WIDE], F32R)
        bw_rows = sb("bw_rows", [ROWS, NT, WIDE], F32R)
        xa_rows = sb("xa_rows", [P, 2, P])
        xa_t = sb("xa_t", [P, 2, P], F32R)
        top_val = sb("top_val", [P, 2, 8])
        top_idx = sb("top_idx", [P, 2, 8], U32)
        top_diff = sb("top_diff", [P, 2, TOP])
        top_exp = sb("top_exp", [P, 2, TOP])
        top_sum = sb("top_sum", [P, 2, 1])
        top_rcp = sb("top_rcp", [P, 2, 1])
        onehot = sb("onehot", [P, 2, TOP, E])
        weighted = sb("weighted", [P, 2, TOP, E])
        route = sb("route", [P, 2, E])
        hw = sb("hw", [P, 2, ER])
        hw_hi = sb("hw_hi", [P, 2, P], F32R)
        hw_lo = sb("hw_lo", [P, 2, P], F32R)
        y_out = sb("y_out", [P, NT, D])
        ident = sb("ident", [P, P])
        expert_id = sb("expert_id", [P, E])

        bank = [ctx.enter_context(nc.psum_tensor(f"bank{i}", [P, 512], F32)) for i in range(8)]
        c_bank = bank[0:4]
        cgh_bank = [bank[4][:, i * GH:(i + 1) * GH] for i in range(3)] + [bank[5][:, 0:GH]]
        g_bank = bank[4:6]
        bw_bank, t2_bank = bank[6], bank[6]
        bwgh_bank, t1_bank = bank[7], bank[7]

        wa_loaded = [sem(f"wa_loaded{m}") for m in range(KC)]
        wb_loaded = [sem(f"wb_loaded{m}") for m in range(KC)]
        x_loaded = [sem(f"x_loaded{t}") for t in range(NT)]
        lora_loaded, ffn_b_loaded, bias_loaded = sem("lora_loaded"), sem("ffn_b_loaded"), sem("bias_loaded")
        ident_zero, ident_ready, const_ready, pads_ready = (
            sem("ident_zero"), sem("ident_ready"), sem("const_ready"), sem("pads_ready"))
        w_hi_done, w_lo_done = sem("w_hi_done"), sem("w_lo_done")
        lb_placed, lb_hi_done, lb_lo_done = sem("lb_placed"), sem("lb_hi_done"), sem("lb_lo_done")
        x_hi_done, x_lo_done = sem("x_hi_done"), sem("x_lo_done")
        ffn_b_hi_done, ffn_b_lo_done = sem("ffn_b_hi_done"), sem("ffn_b_lo_done")
        bias_hi_done, bias_lo_done = sem("bias_hi_done"), sem("bias_lo_done")
        cgh_summed, cgh_copied = sem("cgh_summed"), sem("cgh_copied")
        c_summed, c_plus_i, c_hi_done, c_lo_done = sem("c_summed"), sem("c_plus_i"), sem("c_hi_done"), sem("c_lo_done")
        bw_summed, bw_hi_done, bw_lo_done = sem("bw_summed"), sem("bw_hi_done"), sem("bw_lo_done")
        bw_rows_loaded, bias_rows_loaded, lora_a_placed = sem("bw_rows_loaded"), sem("bias_rows_loaded"), sem("lora_a_placed")
        g_done, xa_hi_done, xa_done, t1_done, xa_t_done = (
            sem("g_done"), sem("xa_hi_done"), sem("xa_done"), sem("t1_done"), sem("xa_t_done"))
        lg_done, lz_done, gate_step, diff_done, exp_done, hw_done = (
            sem("lg_done"), sem("lz_done"), sem("gate_step"), sem("diff_done"), sem("exp_done"), sem("hw_done"))
        t2_done, hw_hi_done, hw_lo_done, z_done, y_done, out_stored = (
            sem("t2_done"), sem("hw_hi_done"), sem("hw_lo_done"), sem("z_done"), sem("y_done"), sem("out_stored"))

        def raw_wt(m):
            return w_raw[:, m, 0:D]

        def raw_gh(m):
            return w_raw[:, m, D:D + GH]

        def raw_wb(m):
            return w_raw[:, m, D + GH:]

        def batch_rows(n):
            return bw_rows[n * R:(n + 1) * R].bitcast(F32)

        def own_cols(t):
            return slice(0, R + GH) if t % 2 == 0 else slice(R, R + GH + R)

        def a_cols(t):
            return slice(0, R) if t % 2 == 0 else slice(R + GH, R + GH + R)

        block = ctx.enter_context(nc.Block())

        @block.sync
        def _(sp):
            for m in range(KC):
                sp.dma_start(w_raw[:, m, 0:D + GH], fold_in[m, :, 0:D + GH]).then_inc(wa_loaded[m], DMA)
                sp.dma_start(w_raw[:, m, D + GH:], fold_in[m, :, D + GH:]).then_inc(wb_loaded[m], DMA)
            for b in range(NT):
                a = sp.value_load(itok[0:1, b:b + 1], min_val=0, max_val=NA - 1)
                sp.dma_start(lora_raw[:, b, :], lora[bass.ds(a, 1), :, :].rearrange("a p c -> (a p) c")).then_inc(lora_loaded, DMA)
            sp.dma_start(bias_raw[:], bias).then_inc(bias_loaded, DMA)
            for t in range(NT):
                sp.dma_start(x_raw[:, t], x_t[t]).then_inc(x_loaded[t], DMA)
            sp.dma_start(ffn_b_raw[:], ffn_b).then_inc(ffn_b_loaded, DMA)

            sp.wait_ge(bw_hi_done, 2)
            for n in range(2):
                sp.dma_start(batch_rows(n), bw_hi[:].bitcast(F32)).then_inc(bw_rows_loaded, DMA)
            sp.wait_ge(bw_lo_done, 2)
            for n in range(2, 4):
                sp.dma_start(batch_rows(n), bw_lo[:].bitcast(F32)).then_inc(bw_rows_loaded, DMA)

            for t in range(NT):
                sp.wait_ge(y_done, t + 1)
                sp.dma_start(out[t], y_out[:, t, :]).then_inc(out_stored, DMA)
            sp.wait_ge(out_stored, NT * DMA)

        @block.gpsimd
        def _(pool):
            nc.gpsimd.memset(ident[:], 0.0).then_inc(ident_zero, 1)
            pool.wait_ge(ident_zero, 1)
            nc.gpsimd.affine_select(out=ident[:], in_=ident[:], compare_op=ALU.not_equal, fill=1.0, base=0,
                                    pattern=[[-1, P]], channel_multiplier=1).then_inc(ident_ready, 1)
            nc.gpsimd.iota(expert_id[:], pattern=[[1, E]], base=0, channel_multiplier=0,
                           allow_small_or_imprecise_dtypes=True).then_inc(const_ready, 1)
            nc.gpsimd.memset(xa_rows[:, :, 4 * R:ROWS], 1.0).then_inc(const_ready, 1)
            nc.gpsimd.memset(xa_rows[:, :, ROWS:], 0.0).then_inc(const_ready, 1)
            pool.wait_ge(const_ready, 3)
            nc.gpsimd.memset(bw_rows[4 * R:ROWS, :, D:].bitcast(F32), 0.0).then_inc(pads_ready, 1)
            pool.wait_ge(pads_ready, 1)
            pool.wait_ge(lora_loaded, NT * DMA)
            nc.gpsimd.tensor_copy(lb_raw[:].rearrange("p c r b -> p b c r"),
                                  lora_raw[:, :, KC * R:].rearrange("p b (c r) -> p b c r", c=KC)).then_inc(lb_placed, 1)
            pool.wait_ge(bias_hi_done, 1)
            pool.wait_ge(bias_lo_done, 1)
            for n, part in enumerate((bias_hi, bias_lo)):
                pool.dma_start(bw_rows[4 * R + n:4 * R + n + 1, :, 0:D].bitcast(F32),
                               part[:].bitcast(F32).unsqueeze(1).broadcast_to([1, NT, D])).then_inc(bias_rows_loaded, DMA)
            pool.wait_ge(lb_placed, 1)
            for t in range(NT):
                if t >= 1:
                    pool.wait_ge(lora_a_placed, t)
                if t >= 2:
                    pool.wait_ge(g_done, t - 1)
                nc.gpsimd.tensor_copy(c_gh[:, :, a_cols(t)],
                                      lora_raw[:, t, 0:KC * R].rearrange("p (c r) -> p c r", c=KC)).then_inc(lora_a_placed, 1)

        @block.scalar
        def _(act):
            for m in range(KC):
                act.wait_ge(wa_loaded[m], DMA)
                nc.scalar.copy(wt_hi[:, m, :], raw_wt(m)).then_inc(w_hi_done, 1)
                act.wait_ge(wb_loaded[m], DMA)
                nc.scalar.copy(wb_hi[:, m, :], raw_wb(m)).then_inc(w_hi_done, 1)
            act.wait_ge(lora_loaded, NT * DMA)
            nc.scalar.copy(lb_hi[:].rearrange("p c r b -> p b c r"),
                           lora_raw[:, :, KC * R:].rearrange("p b (c r) -> p b c r", c=KC)).then_inc(lb_hi_done, 1)
            act.wait_ge(bias_loaded, DMA)
            nc.scalar.copy(bias_hi[:], bias_raw[:]).then_inc(bias_hi_done, 1)
            for t in range(NT):
                act.wait_ge(x_loaded[t], DMA)
                nc.scalar.copy(x_hi[:, t], x_raw[:, t]).then_inc(x_hi_done, 1)
            act.wait_ge(ffn_b_loaded, DMA)
            nc.scalar.copy(ffn_b_hi[:], ffn_b_raw[:]).then_inc(ffn_b_hi_done, 1)
            act.wait_ge(cgh_summed, 1)
            nc.scalar.copy(c_gh[:, 0:3, R:R + GH], bank[4][:, 0:3 * GH].rearrange("p (c n) -> p c n", c=3)).then_inc(cgh_copied, 1)
            nc.scalar.copy(c_gh[:, 3, R:R + GH], cgh_bank[3]).then_inc(cgh_copied, 1)
            act.wait_ge(bw_summed, 1)
            nc.scalar.copy(bw_hi[:, 0:D], bw_bank[:]).then_inc(bw_hi_done, 1)
            nc.scalar.copy(bw_hi[:, D:], bwgh_bank[:, 0:GH]).then_inc(bw_hi_done, 1)
            for i in range(KC):
                act.wait_ge(c_plus_i, i + 1)
                nc.scalar.copy(c_hi[:, i, :], c_bank[i][:]).then_inc(c_hi_done, 1)

            def split_hw(t):
                act.wait_ge(t2_done, t + 1)
                if t >= 2:
                    act.wait_ge(z_done, t - 1)
                nc.scalar.copy(hw_hi[:, t % 2, :], t2_bank[:, 0:P]).then_inc(hw_hi_done, 1)

            def copy_out(t):
                act.wait_ge(z_done, t + 1)
                nc.scalar.copy(y_out[:, t, :], c_bank[t % 4][:]).then_inc(y_done, 1)

            for t in range(NT):
                act.wait_ge(t1_done, t + 1)
                if t >= 2:
                    act.wait_ge(lz_done, t - 1)
                nc.scalar.copy(xa_t[:, t % 2, :], t1_bank[:, 0:P]).then_inc(xa_t_done, 1)
                if t >= 1:
                    split_hw(t - 1)
                act.wait_ge(diff_done, t + 1)
                nc.scalar.activation(top_exp[:, t % 2], top_diff[:, t % 2], ACT.Exp,
                                     accum_out=top_sum[:, t % 2]).then_inc(exp_done, 1)
                if t >= 1:
                    copy_out(t - 1)
            split_hw(NT - 1)
            copy_out(NT - 1)

        @block.vector
        def _(dve):
            def lo(out, raw, hi, done):
                nc.vector.tensor_tensor(out, raw, hi.bitcast(F32), ALU.subtract).then_inc(done, 1)

            for m in range(KC):
                dve.wait_ge(w_hi_done, 2 * m + 1)
                lo(wt_lo[:, m, :], raw_wt(m), wt_hi[:, m, :], w_lo_done)
                dve.wait_ge(w_hi_done, 2 * m + 2)
                lo(wb_lo[:, m, :], raw_wb(m), wb_hi[:, m, :], w_lo_done)
            dve.wait_ge(lb_hi_done, 1)
            dve.wait_ge(lb_placed, 1)
            lo(lb_lo[:], lb_raw[:], lb_hi[:], lb_lo_done)
            dve.wait_ge(bias_hi_done, 1)
            lo(bias_lo[:], bias_raw[:], bias_hi[:], bias_lo_done)
            for t in range(NT):
                dve.wait_ge(x_hi_done, t + 1)
                lo(x_lo[:, t], x_raw[:, t], x_hi[:, t], x_lo_done)
            dve.wait_ge(ffn_b_hi_done, 1)
            lo(ffn_b_lo[:], ffn_b_raw[:], ffn_b_hi[:], ffn_b_lo_done)
            dve.wait_ge(bw_hi_done, 1)
            lo(bw_lo[:, 0:D], bw_bank[:], bw_hi[:, 0:D], bw_lo_done)
            dve.wait_ge(bw_hi_done, 2)
            lo(bw_lo[:, D:], bwgh_bank[:, 0:GH], bw_hi[:, D:], bw_lo_done)
            dve.wait_ge(ident_ready, 1)
            for i in range(KC + 1):
                if i < KC:
                    dve.wait_ge(c_summed, i + 1)
                    diag = c_bank[i][:, i * P:(i + 1) * P]
                    nc.vector.tensor_tensor(diag, diag, ident[:], ALU.add).then_inc(c_plus_i, 1)
                if i >= 1:
                    dve.wait_ge(c_hi_done, i)
                    lo(c_lo[:, i - 1, :], c_bank[i - 1][:], c_hi[:, i - 1, :], c_lo_done)

            steps = [0]

            def step(instruction):
                instruction.then_inc(gate_step, 1)
                steps[0] += 1
                dve.wait_ge(gate_step, steps[0])

            def split_xa(t):
                dve.wait_ge(g_done, t + 1)
                if t >= 2:
                    dve.wait_ge(t1_done, t - 1)
                xa = g_bank[t % 2][:, a_cols(t)].unsqueeze(1).broadcast_to([P, 2, R])
                rows = xa_rows[:, t % 2, 0:4 * R].rearrange("p (n h r) -> p n h r", n=2, h=2)
                nc.vector.tensor_copy(rows[:, :, 0, :].bitcast(F32R), xa).then_inc(xa_hi_done, 1)
                dve.wait_ge(xa_hi_done, t + 1)
                nc.vector.tensor_tensor(rows[:, :, 1, :].bitcast(F32R), xa, rows[:, :, 0, :], ALU.subtract).then_inc(xa_done, 1)

            def split_hw(t):
                dve.wait_ge(hw_hi_done, t + 1)
                if t >= 2:
                    dve.wait_ge(z_done, t - 1)
                lo(hw_lo[:, t % 2, :], t2_bank[:, 0:P], hw_hi[:, t % 2, :], hw_lo_done)

            def gate(t):
                n = t % 2
                logits = g_bank[n][:, R:R + E]
                h = g_bank[n][:, R + E:R + GH].rearrange("p (e r) -> p e r", e=E)
                dve.wait_ge(lg_done, t + 1)
                step(nc.vector.max(top_val[:, n], logits))
                nc.vector.tensor_scalar(top_diff[:, n], top_val[:, n, 0:TOP], top_val[:, n, 0:1], None,
                                        ALU.subtract).then_inc(diff_done, 1)
                step(nc.vector.max_index(top_idx[:, n], top_val[:, n], logits))
                step(nc.vector.tensor_tensor(onehot[:, n], expert_id[:].unsqueeze(1).broadcast_to([P, TOP, E]),
                                             top_idx[:, n, 0:TOP].unsqueeze(2).broadcast_to([P, TOP, E]), ALU.is_equal))
                dve.wait_ge(exp_done, t + 1)
                nc.vector.reciprocal(top_rcp[:, n], top_sum[:, n])
                step(nc.vector.tensor_tensor(weighted[:, n], onehot[:, n],
                                             top_exp[:, n].unsqueeze(2).broadcast_to([P, TOP, E]), ALU.mult))
                step(nc.vector.tensor_tensor(route[:, n], weighted[:, n, 0, :], weighted[:, n, 1, :], ALU.add))
                if t >= 2:
                    dve.wait_ge(t2_done, t - 1)
                nc.vector.scalar_tensor_tensor(out=hw[:, n].rearrange("p (e r) -> p e r", e=E), in0=h,
                                               scalar=top_rcp[:, n], in1=route[:, n].unsqueeze(2).broadcast_to([P, E, R]),
                                               op0=ALU.mult, op1=ALU.mult).then_inc(hw_done, 1)

            dve.wait_ge(const_ready, 3)
            for t in range(NT):
                split_xa(t)
                if t >= 1:
                    split_hw(t - 1)
                gate(t)
            split_hw(NT - 1)

        @block.tensor
        def _(pe):
            def product(out, a_hi, a_lo, b_hi, b_lo, first, last):
                nc.tensor.matmul(out, a_hi, b_hi, start=first, stop=False)
                nc.tensor.matmul(out, a_hi, b_lo, start=False, stop=False)
                return nc.tensor.matmul(out, a_lo, b_hi, start=False, stop=last)

            def fold_gh(m):
                pe.wait_ge(wa_loaded[m], DMA)
                for i in range(KC):
                    mm = nc.tensor.matmul(cgh_bank[i], w_raw[:, m, i * P:(i + 1) * P], raw_gh(m),
                                          start=(m == 0 and i in (0, 3)), stop=(m == KC - 1), skip_group_check=True)
                return mm

            def fold_z(m, i):
                return product(c_bank[i][:], wt_hi[:, m, i * P:(i + 1) * P], wt_lo[:, m, i * P:(i + 1) * P],
                               wb_hi[:, m, :], wb_lo[:, m, :], m == 0, m == KC - 1)

            def G(t):
                n = t % 2
                pe.wait_ge(cgh_copied, 2)
                pe.wait_ge(lora_a_placed, t + 1)
                pe.wait_ge(x_loaded[t], DMA)
                if t >= 2:
                    pe.wait_ge(hw_done, t - 1)
                for c in range(KC):
                    mm = nc.tensor.matmul(g_bank[n][:, own_cols(t)], x_raw[:, t, c, :], c_gh[:, c, own_cols(t)],
                                          start=(c == 0), stop=(c == KC - 1), skip_group_check=True)
                mm.then_inc(g_done, 1)

            def Z(t, chunks):
                pe.wait_ge(x_lo_done, t + 1)
                for c in chunks:
                    pe.wait_ge(c_lo_done, c + 1 if t == 0 else KC)
                    if c == 0 and t < 4:
                        pe.wait_ge(c_lo_done, t + 1)
                    if c == 0 and t >= 4:
                        pe.wait_ge(y_done, t - 3)
                    product(c_bank[t % 4][:], x_hi[:, t, c, :], x_lo[:, t, c, :], c_hi[:, c, :], c_lo[:, c, :], c == 0, False)

            def T1(t):
                pe.wait_ge(xa_done, t + 1)
                if t >= 1:
                    pe.wait_ge(xa_t_done, t)
                nc.tensor.transpose(t1_bank[:, 0:P], xa_rows[:, t % 2, :], ident[:]).then_inc(t1_done, 1)

            def Lg(t):
                pe.wait_ge(xa_t_done, t + 1)
                if t == 0:
                    pe.wait_ge(pads_ready, 1)
                    pe.wait_ge(bw_rows_loaded, 4 * DMA)
                pe.wait_ge(bias_rows_loaded, 2 * DMA)
                nc.tensor.matmul(g_bank[t % 2][:, R:R + GH], xa_t[0:ROWS, t % 2, :], bw_rows[:, t, D:],
                                 start=False, stop=True, skip_group_check=True).then_inc(lg_done, 1)

            def Lz(t):
                nc.tensor.matmul(c_bank[t % 4][:], xa_t[0:ROWS, t % 2, :], bw_rows[:, t, 0:D],
                                 start=False, stop=False).then_inc(lz_done, 1)

            def T2(t):
                pe.wait_ge(hw_done, t + 1)
                if t >= 1:
                    pe.wait_ge(hw_lo_done, t)
                nc.tensor.transpose(t2_bank[:, 0:P], hw[:, t % 2, :], ident[:]).then_inc(t2_done, 1)

            def Dl(t):
                pe.wait_ge(hw_lo_done, t + 1)
                product(c_bank[t % 4][:], hw_hi[:, t % 2, :], hw_lo[:, t % 2, :], ffn_b_hi[:], ffn_b_lo[:],
                        False, True).then_inc(z_done, 1)

            for m in range(KC - 1):
                fold_gh(m)
                pe.wait_ge(w_lo_done, 2 * m + 2)
                for i in range(KC):
                    fold_z(m, i)
            fold_gh(KC - 1).then_inc(cgh_summed, 1)
            pe.wait_ge(lora_loaded, NT * DMA)
            pe.wait_ge(w_lo_done, 2 * KC)
            pe.wait_ge(lb_placed, 1)
            pe.wait_ge(lb_lo_done, 1)
            for m in range(KC):
                nc.tensor.matmul(bwgh_bank[:, 0:GH], lb_raw[:, m].rearrange("p r b -> p (r b)"), raw_gh(m),
                                 start=(m == 0), stop=(m == KC - 1))
            for m in range(KC):
                mm = product(bw_bank[:], lb_hi[:, m].rearrange("p r b -> p (r b)"), lb_lo[:, m].rearrange("p r b -> p (r b)"),
                             wb_hi[:, m, :], wb_lo[:, m, :], m == 0, m == KC - 1)
            mm.then_inc(bw_summed, 1)
            for i in range(KC):
                fold_z(KC - 1, i).then_inc(c_summed, 1)

            pe.wait_ge(ffn_b_lo_done, 1)
            pe.wait_ge(ident_ready, 1)
            pe.wait_ge(const_ready, 3)
            pe.wait_ge(bw_lo_done, 2)
            G(0)
            Z(0, (0, 1))
            T1(0)
            Z(0, (2, 3))
            G(1)
            Z(1, (0, 1))
            Lg(0)
            Lz(0)
            T1(1)
            Z(1, (2, 3))
            T2(0)
            Lg(1)
            Lz(1)
            Dl(0)
            for t in range(2, NT):
                G(t)
                Z(t, (0, 1))
                T1(t)
                T2(t - 1)
                Z(t, (2, 3))
                Lg(t)
                Lz(t)
                Dl(t - 1)
            T2(NT - 1)
            Dl(NT - 1)


def kernel(x, itok_B_0_15, L0_cond_W, L0_cond_lora_A, L0_cond_lora_B, L0_ffn_W_base, L0_ffn_b_base,
           L0_ffn_W_gate, L0_ffn_A, L0_ffn_B):
    import numpy as np
    import concourse.bacc as bacc
    from concourse.bass_utils import run_bass_kernel_spmd

    a = np.asarray

    def chunked(w):
        return a(w).reshape(KC, P, -1)

    fold_in = np.concatenate([chunked(a(L0_cond_W).T), chunked(a(L0_ffn_W_gate).T),
                              chunked(a(L0_ffn_A).reshape(ER, D).T), chunked(a(L0_ffn_W_base).T)], axis=2)
    lora_a = a(L0_cond_lora_A).reshape(NA, KC, P, R).transpose(0, 2, 1, 3).reshape(NA, P, KC * R)
    lora_b = a(L0_cond_lora_B).transpose(0, 2, 1).reshape(NA, KC, P, R).transpose(0, 2, 1, 3).reshape(NA, P, KC * R)
    arrays = {
        "x_t": a(x).reshape(NT, P, KC, P).transpose(0, 3, 2, 1),
        "itok": a(itok_B_0_15).reshape(1, NT),
        "fold_in": fold_in,
        "lora": np.concatenate([lora_a, lora_b], axis=2),
        "ffn_b": a(L0_ffn_B).transpose(0, 2, 1).reshape(ER, D),
        "bias": a(L0_ffn_b_base).reshape(1, D),
    }
    arrays = {name: np.ascontiguousarray(v) for name, v in arrays.items()}
    nc = bacc.Bacc("TRN2", target_bir_lowering=False, num_devices=1)
    args = [nc.dram_tensor(name, v.shape, mybir.dt.from_np(v.dtype), kind="ExternalInput").ap()
            for name, v in arrays.items()]
    out = nc.dram_tensor("out", (NT, P, D), F32, kind="ExternalOutput").ap()
    adaln_ffn_kernel(nc, *args, out)
    result = run_bass_kernel_spmd(nc, [arrays], core_ids=[0])
    return result.results[0]["out"]
```

```python
from contextlib import ExitStack

import concourse.bass as bass
from concourse import mybir

F32 = mybir.dt.float32
F32R = mybir.dt.float32r
U32 = mybir.dt.uint32
ALU = mybir.AluOpType
ACT = mybir.ActivationFunctionType

P = 128
NT = 8
D = 512
KC = D // P
R = 16
NA = 16
E = 8
ER = E * R
GH = E + ER
WIDE = D + GH
TOP = 2
ROWS = 4 * R + 2
WARM_UPS = 24
X_EARLY = 4
DMA = 16


def adaln_ffn_kernel(nc, x_t, itok, fold_in, lora, ffn_b, bias, out):
    ctx = ExitStack()
    with ctx:
        def sb(name, shape, dt=F32):
            return ctx.enter_context(nc.sbuf_tensor(name, shape, dt))

        def sem(name):
            return ctx.enter_context(nc.semaphore(name))

        w_raw = sb("w_raw", [P, KC, D + GH + D])
        lora_raw = sb("lora_raw", [P, NT, 2 * KC * R])
        x_raw = sb("x_raw", [P, NT, KC, P])
        ffn_b_raw = sb("ffn_b_raw", [P, D])
        bias_raw = sb("bias_raw", [1, D])
        wt_hi = sb("wt_hi", [P, KC, D], F32R)
        wt_lo = sb("wt_lo", [P, KC, D], F32R)
        wb_hi = sb("wb_hi", [P, KC, D], F32R)
        wb_lo = sb("wb_lo", [P, KC, D], F32R)
        lb_raw = sb("lb_raw", [P, KC, R, NT])
        lb_hi = sb("lb_hi", [P, KC, R, NT], F32R)
        lb_lo = sb("lb_lo", [P, KC, R, NT], F32R)
        x_hi = sb("x_hi", [P, NT, KC, P], F32R)
        x_lo = sb("x_lo", [P, NT, KC, P], F32R)
        ffn_b_hi = sb("ffn_b_hi", [P, D], F32R)
        ffn_b_lo = sb("ffn_b_lo", [P, D], F32R)
        bias_hi = sb("bias_hi", [1, D], F32R)
        bias_lo = sb("bias_lo", [1, D], F32R)
        c_hi = sb("c_hi", [P, KC, D], F32R)
        c_lo = sb("c_lo", [P, KC, D], F32R)
        c_gh = sb("c_gh", [P, KC, R + GH + R])
        bw_hi = sb("bw_hi", [P, WIDE], F32R)
        bw_lo = sb("bw_lo", [P, WIDE], F32R)
        bw_rows = sb("bw_rows", [ROWS, NT, WIDE], F32R)
        xa_rows = sb("xa_rows", [P, 2, P])
        xa_t = sb("xa_t", [P, 2, P], F32R)
        top_val = sb("top_val", [P, 2, 8])
        top_idx = sb("top_idx", [P, 2, 8], U32)
        top_diff = sb("top_diff", [P, 2, TOP])
        top_exp = sb("top_exp", [P, 2, TOP])
        top_sum = sb("top_sum", [P, 2, 1])
        top_rcp = sb("top_rcp", [P, 2, 1])
        onehot = sb("onehot", [P, 2, TOP, E])
        weighted = sb("weighted", [P, 2, TOP, E])
        route = sb("route", [P, 2, E])
        hw = sb("hw", [P, 2, ER])
        hw_hi = sb("hw_hi", [P, 2, P], F32R)
        hw_lo = sb("hw_lo", [P, 2, P], F32R)
        y_out = sb("y_out", [P, NT, D])
        zeros = sb("zeros", [P, P // 2])
        ident = sb("ident", [P, P])
        expert_id = sb("expert_id", [P, E])

        bank = [ctx.enter_context(nc.psum_tensor(f"bank{i}", [P, 512], F32)) for i in range(8)]
        c_bank = bank[0:4]
        cgh_bank = [bank[4][:, i * GH:(i + 1) * GH] for i in range(3)] + [bank[5][:, 0:GH]]
        g_bank = bank[4:6]
        bw_bank, t2_bank = bank[6], bank[6]
        bwgh_bank, t1_bank = bank[7], bank[7]

        wa_loaded = [sem(f"wa_loaded{m}") for m in range(KC)]
        wb_loaded = [sem(f"wb_loaded{m}") for m in range(KC)]
        x_loaded = [sem(f"x_loaded{t}") for t in range(NT)]
        lora_loaded, ffn_b_loaded, bias_loaded = sem("lora_loaded"), sem("ffn_b_loaded"), sem("bias_loaded")
        zeros_ready = sem("zeros_ready")
        ident_zero, ident_ready, const_ready, pads_ready = (
            sem("ident_zero"), sem("ident_ready"), sem("const_ready"), sem("pads_ready"))
        w_hi_done, w_lo_done = sem("w_hi_done"), sem("w_lo_done")
        lb_placed, lb_hi_done, lb_lo_done = sem("lb_placed"), sem("lb_hi_done"), sem("lb_lo_done")
        x_hi_done, x_lo_done = sem("x_hi_done"), sem("x_lo_done")
        ffn_b_hi_done, ffn_b_lo_done = sem("ffn_b_hi_done"), sem("ffn_b_lo_done")
        bias_hi_done, bias_lo_done = sem("bias_hi_done"), sem("bias_lo_done")
        cgh_summed, cgh_copied = sem("cgh_summed"), sem("cgh_copied")
        c_summed, c_plus_i, c_hi_done, c_lo_done = sem("c_summed"), sem("c_plus_i"), sem("c_hi_done"), sem("c_lo_done")
        bw_summed, bw_hi_done, bw_lo_done = sem("bw_summed"), sem("bw_hi_done"), sem("bw_lo_done")
        bw_rows_loaded, bias_rows_loaded, lora_a_placed = sem("bw_rows_loaded"), sem("bias_rows_loaded"), sem("lora_a_placed")
        g_done, xa_hi_done, xa_done, t1_done, xa_t_done = (
            sem("g_done"), sem("xa_hi_done"), sem("xa_done"), sem("t1_done"), sem("xa_t_done"))
        lg_done, lz_done, gate_step, diff_done, exp_done, hw_done = (
            sem("lg_done"), sem("lz_done"), sem("gate_step"), sem("diff_done"), sem("exp_done"), sem("hw_done"))
        t2_done, hw_hi_done, hw_lo_done, z_done, y_done, out_stored = (
            sem("t2_done"), sem("hw_hi_done"), sem("hw_lo_done"), sem("z_done"), sem("y_done"), sem("out_stored"))

        def raw_wt(m):
            return w_raw[:, m, 0:D]

        def raw_gh(m):
            return w_raw[:, m, D:D + GH]

        def raw_wb(m):
            return w_raw[:, m, D + GH:]

        def batch_rows(n):
            return bw_rows[n * R:(n + 1) * R].bitcast(F32)

        def own_cols(t):
            return slice(0, R + GH) if t % 2 == 0 else slice(R, R + GH + R)

        def a_cols(t):
            return slice(0, R) if t % 2 == 0 else slice(R + GH, R + GH + R)

        block = ctx.enter_context(nc.Block())

        @block.sync
        def _(sp):
            def load_fold(m):
                sp.dma_start(w_raw[:, m, 0:D + GH], fold_in[m, :, 0:D + GH]).then_inc(wa_loaded[m], DMA)
                sp.dma_start(w_raw[:, m, D + GH:], fold_in[m, :, D + GH:]).then_inc(wb_loaded[m], DMA)

            for m in range(KC - 1):
                load_fold(m)
            _, adapters = nc.values_load_multi_w_load_instructions(
                itok[0:1, :], engines=[mybir.EngineType.SP], min_val=0, max_val=NA - 1)
            load_fold(KC - 1)
            for b in range(NT):
                sp.dma_start(lora_raw[:, b, :], lora[bass.ds(adapters[b], 1), :, :].rearrange("a p c -> (a p) c")).then_inc(lora_loaded, DMA)
            sp.dma_start(bias_raw[:], bias).then_inc(bias_loaded, DMA)
            for t in range(NT):
                sp.dma_start(x_raw[:, t], x_t[t]).then_inc(x_loaded[t], DMA)
            sp.dma_start(ffn_b_raw[:], ffn_b).then_inc(ffn_b_loaded, DMA)

            sp.wait_ge(bw_hi_done, 2)
            for n in range(2):
                sp.dma_start(batch_rows(n), bw_hi[:].bitcast(F32)).then_inc(bw_rows_loaded, DMA)
            sp.wait_ge(bw_lo_done, 2)
            for n in range(2, 4):
                sp.dma_start(batch_rows(n), bw_lo[:].bitcast(F32)).then_inc(bw_rows_loaded, DMA)

            for t in range(NT):
                sp.wait_ge(y_done, t + 1)
                cols = D if t + 1 < NT else D // 2
                sp.dma_start(out[t, :, 0:cols], y_out[:, t, 0:cols]).then_inc(out_stored, DMA)
            sp.wait_ge(out_stored, (NT + 1) * DMA)

        @block.gpsimd
        def _(pool):
            nc.gpsimd.memset(ident[:], 0.0).then_inc(ident_zero, 1)
            pool.wait_ge(ident_zero, 1)
            nc.gpsimd.affine_select(out=ident[:], in_=ident[:], compare_op=ALU.not_equal, fill=1.0, base=0,
                                    pattern=[[-1, P]], channel_multiplier=1).then_inc(ident_ready, 1)
            nc.gpsimd.iota(expert_id[:], pattern=[[1, E]], base=0, channel_multiplier=0,
                           allow_small_or_imprecise_dtypes=True).then_inc(const_ready, 1)
            nc.gpsimd.memset(xa_rows[:, :, 4 * R:ROWS], 1.0).then_inc(const_ready, 1)
            nc.gpsimd.memset(xa_rows[:, :, ROWS:], 0.0).then_inc(const_ready, 1)
            pool.wait_ge(const_ready, 3)
            nc.gpsimd.memset(bw_rows[4 * R:ROWS, :, D:].bitcast(F32), 0.0).then_inc(pads_ready, 1)
            pool.wait_ge(pads_ready, 1)
            pool.wait_ge(lora_loaded, NT * DMA)
            nc.gpsimd.tensor_copy(lb_raw[:].rearrange("p c r b -> p b c r"),
                                  lora_raw[:, :, KC * R:].rearrange("p b (c r) -> p b c r", c=KC)).then_inc(lb_placed, 1)
            pool.wait_ge(bias_hi_done, 1)
            pool.wait_ge(bias_lo_done, 1)
            for n, part in enumerate((bias_hi, bias_lo)):
                pool.dma_start(bw_rows[4 * R + n:4 * R + n + 1, :, 0:D].bitcast(F32),
                               part[:].bitcast(F32).unsqueeze(1).broadcast_to([1, NT, D])).then_inc(bias_rows_loaded, DMA)
            pool.wait_ge(lb_placed, 1)
            for t in range(NT):
                if t >= 1:
                    pool.wait_ge(lora_a_placed, t)
                if t >= 2:
                    pool.wait_ge(g_done, t - 1)
                nc.gpsimd.tensor_copy(c_gh[:, :, a_cols(t)],
                                      lora_raw[:, t, 0:KC * R].rearrange("p (c r) -> p c r", c=KC)).then_inc(lora_a_placed, 1)

        @block.scalar
        def _(act):
            for m in range(KC):
                act.wait_ge(wa_loaded[m], DMA)
                nc.scalar.copy(wt_hi[:, m, :], raw_wt(m)).then_inc(w_hi_done, 1)
                act.wait_ge(wb_loaded[m], DMA)
                nc.scalar.copy(wb_hi[:, m, :], raw_wb(m)).then_inc(w_hi_done, 1)
            act.wait_ge(lora_loaded, NT * DMA)
            nc.scalar.copy(lb_hi[:].rearrange("p c r b -> p b c r"),
                           lora_raw[:, :, KC * R:].rearrange("p b (c r) -> p b c r", c=KC)).then_inc(lb_hi_done, 1)
            act.wait_ge(bias_loaded, DMA)
            nc.scalar.copy(bias_hi[:], bias_raw[:]).then_inc(bias_hi_done, 1)

            def split_x(t):
                act.wait_ge(x_loaded[t], DMA)
                nc.scalar.copy(x_hi[:, t], x_raw[:, t]).then_inc(x_hi_done, 1)

            for t in range(X_EARLY):
                split_x(t)
            act.wait_ge(cgh_summed, 1)
            nc.scalar.copy(c_gh[:, 0:3, R:R + GH], bank[4][:, 0:3 * GH].rearrange("p (c n) -> p c n", c=3)).then_inc(cgh_copied, 1)
            nc.scalar.copy(c_gh[:, 3, R:R + GH], cgh_bank[3]).then_inc(cgh_copied, 1)
            act.wait_ge(bw_summed, 1)
            nc.scalar.copy(bw_hi[:, 0:D], bw_bank[:]).then_inc(bw_hi_done, 1)
            nc.scalar.copy(bw_hi[:, D:], bwgh_bank[:, 0:GH]).then_inc(bw_hi_done, 1)
            for i in range(KC):
                act.wait_ge(c_plus_i, i + 1)
                nc.scalar.copy(c_hi[:, i, :], c_bank[i][:]).then_inc(c_hi_done, 1)
            act.wait_ge(ffn_b_loaded, DMA)
            nc.scalar.copy(ffn_b_hi[:], ffn_b_raw[:]).then_inc(ffn_b_hi_done, 1)

            def split_hw(t):
                act.wait_ge(t2_done, t + 1)
                if t >= 2:
                    act.wait_ge(z_done, t - 1)
                nc.scalar.copy(hw_hi[:, t % 2, :], t2_bank[:, 0:P]).then_inc(hw_hi_done, 1)

            def exp_top(t):
                act.wait_ge(diff_done, t + 1)
                nc.scalar.activation(top_exp[:, t % 2], top_diff[:, t % 2], ACT.Exp,
                                     accum_out=top_sum[:, t % 2]).then_inc(exp_done, 1)

            def copy_out(t, parts=1):
                act.wait_ge(z_done, t + 1)
                for n in range(parts):
                    cols = slice(n * D // parts, (n + 1) * D // parts)
                    nc.scalar.copy(y_out[:, t, cols], c_bank[t % 4][:, cols]).then_inc(y_done, 1)

            def copy_xa_t(t):
                act.wait_ge(t1_done, t + 1)
                if t >= 2:
                    act.wait_ge(lz_done, t - 1)
                nc.scalar.copy(xa_t[:, t % 2, :], t1_bank[:, 0:P]).then_inc(xa_t_done, 1)

            copy_xa_t(0)
            exp_top(0)
            copy_xa_t(1)
            exp_top(1)
            split_hw(0)
            copy_xa_t(2)
            copy_out(0)
            for t in range(2, NT):
                split_hw(t - 1)
                exp_top(t)
                if t + X_EARLY - 2 < NT:
                    split_x(t + X_EARLY - 2)
                if t + 1 < NT:
                    copy_out(t - 1)
                    copy_xa_t(t + 1)
            split_hw(NT - 1)
            copy_out(NT - 2)
            copy_out(NT - 1, 2)
            act.wait_ge(y_done, NT + 1)
            act.dma_start(out[NT - 1, :, D // 2:], y_out[:, NT - 1, D // 2:]).then_inc(out_stored, DMA)

        @block.vector
        def _(dve):
            nc.vector.memset(zeros[:], 0.0).then_inc(zeros_ready, 1)

            def lo(out, raw, hi, done):
                nc.vector.tensor_tensor(out, raw, hi.bitcast(F32), ALU.subtract).then_inc(done, 1)

            for m in range(KC):
                dve.wait_ge(w_hi_done, 2 * m + 1)
                lo(wt_lo[:, m, :], raw_wt(m), wt_hi[:, m, :], w_lo_done)
                dve.wait_ge(w_hi_done, 2 * m + 2)
                lo(wb_lo[:, m, :], raw_wb(m), wb_hi[:, m, :], w_lo_done)
            dve.wait_ge(lb_hi_done, 1)
            dve.wait_ge(lb_placed, 1)
            lo(lb_lo[:], lb_raw[:], lb_hi[:], lb_lo_done)
            dve.wait_ge(bias_hi_done, 1)
            lo(bias_lo[:], bias_raw[:], bias_hi[:], bias_lo_done)

            def split_x(t):
                dve.wait_ge(x_hi_done, t + 1)
                lo(x_lo[:, t], x_raw[:, t], x_hi[:, t], x_lo_done)

            for t in range(X_EARLY):
                split_x(t)
            dve.wait_ge(bw_hi_done, 1)
            lo(bw_lo[:, 0:D], bw_bank[:], bw_hi[:, 0:D], bw_lo_done)
            dve.wait_ge(ident_ready, 1)
            for i in range(KC + 1):
                if i == 1:
                    dve.wait_ge(bw_hi_done, 2)
                    lo(bw_lo[:, D:], bwgh_bank[:, 0:GH], bw_hi[:, D:], bw_lo_done)
                if i < KC:
                    dve.wait_ge(c_summed, i + 1)
                    diag = c_bank[i][:, i * P:(i + 1) * P]
                    nc.vector.tensor_tensor(diag, diag, ident[:], ALU.add).then_inc(c_plus_i, 1)
                if i >= 1:
                    dve.wait_ge(c_hi_done, i)
                    lo(c_lo[:, i - 1, :], c_bank[i - 1][:], c_hi[:, i - 1, :], c_lo_done)

            steps = [0]

            def step(instruction):
                instruction.then_inc(gate_step, 1)
                steps[0] += 1
                dve.wait_ge(gate_step, steps[0])

            def split_xa(t):
                dve.wait_ge(g_done, t + 1)
                if t >= 2:
                    dve.wait_ge(t1_done, t - 1)
                xa = g_bank[t % 2][:, a_cols(t)].unsqueeze(1).broadcast_to([P, 2, R])
                rows = xa_rows[:, t % 2, 0:4 * R].rearrange("p (n h r) -> p n h r", n=2, h=2)
                nc.vector.tensor_copy(rows[:, :, 0, :].bitcast(F32R), xa).then_inc(xa_hi_done, 1)
                dve.wait_ge(xa_hi_done, t + 1)
                nc.vector.tensor_tensor(rows[:, :, 1, :].bitcast(F32R), xa, rows[:, :, 0, :], ALU.subtract).then_inc(xa_done, 1)

            def split_hw(t):
                dve.wait_ge(hw_hi_done, t + 1)
                if t >= 2:
                    dve.wait_ge(z_done, t - 1)
                lo(hw_lo[:, t % 2, :], t2_bank[:, 0:P], hw_hi[:, t % 2, :], hw_lo_done)

            def gate(t):
                n = t % 2
                logits = g_bank[n][:, R:R + E]
                h = g_bank[n][:, R + E:R + GH].rearrange("p (e r) -> p e r", e=E)
                dve.wait_ge(lg_done, t + 1)
                step(nc.vector.max(top_val[:, n], logits))
                nc.vector.tensor_scalar(top_diff[:, n], top_val[:, n, 0:TOP], top_val[:, n, 0:1], None,
                                        ALU.subtract).then_inc(diff_done, 1)
                step(nc.vector.max_index(top_idx[:, n], top_val[:, n], logits))
                step(nc.vector.tensor_tensor(onehot[:, n], expert_id[:].unsqueeze(1).broadcast_to([P, TOP, E]),
                                             top_idx[:, n, 0:TOP].unsqueeze(2).broadcast_to([P, TOP, E]), ALU.is_equal))
                dve.wait_ge(exp_done, t + 1)
                nc.vector.reciprocal(top_rcp[:, n], top_sum[:, n])
                step(nc.vector.tensor_tensor(weighted[:, n], onehot[:, n],
                                             top_exp[:, n].unsqueeze(2).broadcast_to([P, TOP, E]), ALU.mult))
                step(nc.vector.tensor_tensor(route[:, n], weighted[:, n, 0, :], weighted[:, n, 1, :], ALU.add))
                if t >= 2:
                    dve.wait_ge(t2_done, t - 1)
                nc.vector.scalar_tensor_tensor(out=hw[:, n].rearrange("p (e r) -> p e r", e=E), in0=h,
                                               scalar=top_rcp[:, n], in1=route[:, n].unsqueeze(2).broadcast_to([P, E, R]),
                                               op0=ALU.mult, op1=ALU.mult).then_inc(hw_done, 1)

            dve.wait_ge(const_ready, 3)
            split_xa(0)
            dve.wait_ge(ffn_b_hi_done, 1)
            lo(ffn_b_lo[:], ffn_b_raw[:], ffn_b_hi[:], ffn_b_lo_done)
            split_xa(1)
            for t in range(NT):
                if t >= 2:
                    split_hw(t - 1)
                gate(t)
                if t == 1:
                    split_hw(t - 1)
                if 2 <= t and t + X_EARLY - 2 < NT:
                    split_x(t + X_EARLY - 2)
                if 1 <= t < NT - 1:
                    split_xa(t + 1)
            split_hw(NT - 1)

        @block.tensor
        def _(pe):
            def product(out, a_hi, a_lo, b_hi, b_lo, first, last):
                nc.tensor.matmul(out, a_hi, b_hi, start=first, stop=False)
                nc.tensor.matmul(out, a_hi, b_lo, start=False, stop=False)
                return nc.tensor.matmul(out, a_lo, b_hi, start=False, stop=last)

            def fold_gh(m):
                pe.wait_ge(wa_loaded[m], DMA)
                for i in range(KC):
                    mm = nc.tensor.matmul(cgh_bank[i], w_raw[:, m, i * P:(i + 1) * P], raw_gh(m),
                                          start=(m == 0 and i in (0, 3)), stop=(m == KC - 1), skip_group_check=True)
                return mm

            def fold_z(m, i):
                return product(c_bank[i][:], wt_hi[:, m, i * P:(i + 1) * P], wt_lo[:, m, i * P:(i + 1) * P],
                               wb_hi[:, m, :], wb_lo[:, m, :], m == 0, m == KC - 1)

            def G(t):
                n = t % 2
                pe.wait_ge(cgh_copied, 2)
                pe.wait_ge(lora_a_placed, t + 1)
                pe.wait_ge(x_loaded[t], DMA)
                if t >= 2:
                    pe.wait_ge(hw_done, t - 1)
                for c in range(KC):
                    mm = nc.tensor.matmul(g_bank[n][:, own_cols(t)], x_raw[:, t, c, :], c_gh[:, c, own_cols(t)],
                                          start=(c == 0), stop=(c == KC - 1), skip_group_check=True)
                mm.then_inc(g_done, 1)

            def Z(t, chunks):
                pe.wait_ge(x_lo_done, t + 1)
                for c in chunks:
                    pe.wait_ge(c_lo_done, c + 1 if t == 0 else KC)
                    if c == 0 and t < 4:
                        pe.wait_ge(c_lo_done, t + 1)
                    if c == 0 and t >= 4:
                        pe.wait_ge(y_done, t - 3)
                    product(c_bank[t % 4][:], x_hi[:, t, c, :], x_lo[:, t, c, :], c_hi[:, c, :], c_lo[:, c, :], c == 0, False)

            def T1(t):
                pe.wait_ge(xa_done, t + 1)
                if t == 0:
                    pe.wait_ge(ident_ready, 1)
                    pe.wait_ge(const_ready, 3)
                    pe.wait_ge(bw_lo_done, 2)
                if t >= 1:
                    pe.wait_ge(xa_t_done, t)
                nc.tensor.transpose(t1_bank[:, 0:P], xa_rows[:, t % 2, :], ident[:]).then_inc(t1_done, 1)

            def Lg(t):
                pe.wait_ge(xa_t_done, t + 1)
                if t == 0:
                    pe.wait_ge(pads_ready, 1)
                    pe.wait_ge(bw_rows_loaded, 4 * DMA)
                pe.wait_ge(bias_rows_loaded, 2 * DMA)
                nc.tensor.matmul(g_bank[t % 2][:, R:R + GH], xa_t[0:ROWS, t % 2, :], bw_rows[:, t, D:],
                                 start=False, stop=True, skip_group_check=True).then_inc(lg_done, 1)

            def Lz(t):
                nc.tensor.matmul(c_bank[t % 4][:], xa_t[0:ROWS, t % 2, :], bw_rows[:, t, 0:D],
                                 start=False, stop=False).then_inc(lz_done, 1)

            def T2(t):
                pe.wait_ge(hw_done, t + 1)
                if t >= 1:
                    pe.wait_ge(hw_lo_done, t)
                nc.tensor.transpose(t2_bank[:, 0:P], hw[:, t % 2, :], ident[:]).then_inc(t2_done, 1)

            def Dl(t):
                if t == 0:
                    pe.wait_ge(ffn_b_lo_done, 1)
                pe.wait_ge(hw_lo_done, t + 1)
                product(c_bank[t % 4][:], hw_hi[:, t % 2, :], hw_lo[:, t % 2, :], ffn_b_hi[:], ffn_b_lo[:],
                        False, True).then_inc(z_done, 1)

            pe.wait_ge(zeros_ready, 1)
            for _ in range(WARM_UPS):
                nc.tensor.matmul(bwgh_bank[:, 0:P], zeros[:].bitcast(mybir.dt.bfloat16), zeros[:].bitcast(mybir.dt.bfloat16),
                                 start=True, stop=True)
            for m in range(KC - 1):
                fold_gh(m)
                pe.wait_ge(w_hi_done, 2 * m + 2)
                for i in range(KC):
                    nc.tensor.matmul(c_bank[i][:], wt_hi[:, m, i * P:(i + 1) * P], wb_hi[:, m, :], start=(m == 0), stop=False)
                pe.wait_ge(w_lo_done, 2 * m + 1)
                for i in range(KC):
                    nc.tensor.matmul(c_bank[i][:], wt_lo[:, m, i * P:(i + 1) * P], wb_hi[:, m, :], start=False, stop=False)
                pe.wait_ge(w_lo_done, 2 * m + 2)
                for i in range(KC):
                    nc.tensor.matmul(c_bank[i][:], wt_hi[:, m, i * P:(i + 1) * P], wb_lo[:, m, :], start=False, stop=False)
            fold_gh(KC - 1).then_inc(cgh_summed, 1)
            pe.wait_ge(lora_loaded, NT * DMA)
            pe.wait_ge(w_lo_done, 2 * KC)
            pe.wait_ge(lb_placed, 1)
            pe.wait_ge(lb_lo_done, 1)
            for m in range(KC):
                nc.tensor.matmul(bwgh_bank[:, 0:GH], lb_raw[:, m].rearrange("p r b -> p (r b)"), raw_gh(m),
                                 start=(m == 0), stop=(m == KC - 1))
            for m in range(KC):
                mm = product(bw_bank[:], lb_hi[:, m].rearrange("p r b -> p (r b)"), lb_lo[:, m].rearrange("p r b -> p (r b)"),
                             wb_hi[:, m, :], wb_lo[:, m, :], m == 0, m == KC - 1)
            mm.then_inc(bw_summed, 1)
            for i in range(KC):
                fold_z(KC - 1, i).then_inc(c_summed, 1)

            G(0)
            Z(0, (0, 1, 2, 3))
            T1(0)
            G(1)
            Lg(0)
            Lz(0)
            Z(1, (0,))
            T1(1)
            Z(1, (1,))
            Lg(1)
            Z(1, (2,))
            T2(0)
            Z(1, (3,))
            G(2)
            Lz(1)
            Dl(0)
            T1(2)
            for t in range(2, NT):
                T2(t - 1)
                Z(t, (0,))
                Lg(t)
                Z(t, (1, 2))
                Dl(t - 1)
                if t + 1 < NT:
                    G(t + 1)
                    Z(t, (3,))
                    Lz(t)
                    T1(t + 1)
            T2(NT - 1)
            Lz(NT - 1)
            Z(NT - 1, (3,))
            Dl(NT - 1)


def kernel(x, itok_B_0_15, L0_cond_W, L0_cond_lora_A, L0_cond_lora_B, L0_ffn_W_base, L0_ffn_b_base,
           L0_ffn_W_gate, L0_ffn_A, L0_ffn_B):
    import numpy as np
    import concourse.bacc as bacc
    from concourse.bass_utils import run_bass_kernel_spmd

    a = np.asarray

    def chunked(w):
        return a(w).reshape(KC, P, -1)

    fold_in = np.concatenate([chunked(a(L0_cond_W).T), chunked(a(L0_ffn_W_gate).T),
                              chunked(a(L0_ffn_A).reshape(ER, D).T), chunked(a(L0_ffn_W_base).T)], axis=2)
    lora_a = a(L0_cond_lora_A).reshape(NA, KC, P, R).transpose(0, 2, 1, 3).reshape(NA, P, KC * R)
    lora_b = a(L0_cond_lora_B).transpose(0, 2, 1).reshape(NA, KC, P, R).transpose(0, 2, 1, 3).reshape(NA, P, KC * R)
    arrays = {
        "x_t": a(x).reshape(NT, P, KC, P).transpose(0, 3, 2, 1),
        "itok": a(itok_B_0_15).reshape(1, NT),
        "fold_in": fold_in,
        "lora": np.concatenate([lora_a, lora_b], axis=2),
        "ffn_b": a(L0_ffn_B).transpose(0, 2, 1).reshape(ER, D),
        "bias": a(L0_ffn_b_base).reshape(1, D),
    }
    arrays = {name: np.ascontiguousarray(v) for name, v in arrays.items()}
    nc = bacc.Bacc("TRN2", target_bir_lowering=False, num_devices=1)
    args = [nc.dram_tensor(name, v.shape, mybir.dt.from_np(v.dtype), kind="ExternalInput").ap()
            for name, v in arrays.items()]
    out = nc.dram_tensor("out", (NT, P, D), F32, kind="ExternalOutput").ap()
    adaln_ffn_kernel(nc, *args, out)
    result = run_bass_kernel_spmd(nc, [arrays], core_ids=[0])
    return result.results[0]["out"]
```
